# Optimizing a Trainium2 kernel written in Bass

```python
import numpy as np
import jax
import jax.numpy as jnp

def _softmax(x, axis=-1):
    return jax.nn.softmax(x, axis=axis)

def _gelu(x):
    return jax.nn.gelu(x, approximate=True)

def _silu(x):
    return jax.nn.silu(x)

def _sigmoid(x):
    return jax.nn.sigmoid(x)

def _layernorm(x, axis=-1, eps=1e-05):
    m = jnp.mean(x, axis=axis, keepdims=True)
    v = jnp.var(x, axis=axis, keepdims=True)
    return (x - m) / jnp.sqrt(v + eps)

def _scatter_add(tgt, idx, src, axis=0):
    return tgt.at[idx].add(src)

def _segment_sum(src, seg, n):
    return jax.ops.segment_sum(src, seg, n)
kernel_name = 'mk_rec_standalone_d1_rec_r8_ecd686'

def setup_inputs(seed: int=0):
    np.random.seed(seed)
    _w = jnp.asarray

    def _rec_inputs():
        import jax
        import jax.numpy as jnp
        _rk = jax.random.key(seed)
        r_x = jax.random.randint(jax.random.fold_in(_rk, 1), (2500,), 0, 2500, jnp.int32)
        return r_x
    r_x = _rec_inputs()

    def _L0_rec_setup():
        import jax, jax.numpy as jnp
        import numpy as np
        N_NODES = 2500
        N_EDGES = 40000
        D_EMB = 1024
        N_HID = 1024
        N_CLASS = 40

        def _spmm(row, col, val, x):
            msg = val[:, None] * x[col]
            return jax.ops.segment_sum(msg, row, num_segments=N_NODES)

        def _ngcf_layer(row, col, val, x, W1, W2):
            support = _spmm(row, col, val, x)
            return support @ W1 + support * x @ W2
        key = jax.random.key(seed)
        ks = jax.random.split(key, 10)
        x = jnp.arange(N_NODES, dtype=jnp.int64)
        edge_row = jax.random.randint(ks[0], (N_EDGES,), 0, N_NODES, dtype=jnp.int32)
        edge_col = jax.random.randint(ks[1], (N_EDGES,), 0, N_NODES, dtype=jnp.int32)
        edge_val = jax.random.uniform(ks[2], (N_EDGES,), dtype=jnp.float32)
        emb = jax.random.normal(ks[3], (N_NODES, D_EMB), dtype=jnp.float32) * 0.02
        s1 = 1.0 / np.sqrt(D_EMB)
        s2 = 1.0 / np.sqrt(N_HID)
        W1a = jax.random.normal(ks[4], (D_EMB, N_HID), dtype=jnp.float32) * s1
        W2a = jax.random.normal(ks[5], (D_EMB, N_HID), dtype=jnp.float32) * s1
        W1h = jax.random.normal(ks[6], (D_EMB, N_HID), dtype=jnp.float32) * s1
        W2h = jax.random.normal(ks[7], (D_EMB, N_HID), dtype=jnp.float32) * s1
        W1o = jax.random.normal(ks[8], (N_HID, N_CLASS), dtype=jnp.float32) * s2
        W2o = jax.random.normal(ks[9], (N_HID, N_CLASS), dtype=jnp.float32) * s2
        return {'x': x, 'edge_row': edge_row, 'edge_col': edge_col, 'edge_val': edge_val, 'emb': emb, 'W1a': W1a, 'W2a': W2a, 'W1h': W1h, 'W2h': W2h, 'W1o': W1o, 'W2o': W2o}
    _L0_rec_all = _L0_rec_setup()
    _L0_rec_in = {k: v for k, v in _L0_rec_all.items() if k in ('edge_row', 'edge_col', 'edge_val', 'emb', 'W1a', 'W2a', 'W1h', 'W2h', 'W1o', 'W2o')}
    del _L0_rec_all
    return {'r_x': r_x, 'L0_rec_edge_row': _L0_rec_in['edge_row'], 'L0_rec_edge_col': _L0_rec_in['edge_col'], 'L0_rec_edge_val': _L0_rec_in['edge_val'], 'L0_rec_emb': _L0_rec_in['emb'], 'L0_rec_W1a': _L0_rec_in['W1a'], 'L0_rec_W2a': _L0_rec_in['W2a'], 'L0_rec_W1h': _L0_rec_in['W1h'], 'L0_rec_W2h': _L0_rec_in['W2h'], 'L0_rec_W1o': _L0_rec_in['W1o'], 'L0_rec_W2o': _L0_rec_in['W2o']}

def reference(r_x, L0_rec_edge_row, L0_rec_edge_col, L0_rec_edge_val, L0_rec_emb, L0_rec_W1a, L0_rec_W2a, L0_rec_W1h, L0_rec_W2h, L0_rec_W1o, L0_rec_W2o):
    import jax
    import jax.numpy as jnp

    def _L0_rec_ref(x, edge_row, edge_col, edge_val, emb, W1a, W2a, W1h, W2h, W1o, W2o):
        import jax, jax.numpy as jnp
        import numpy as np
        N_NODES = 2500
        N_EDGES = 40000
        D_EMB = 1024
        N_HID = 1024
        N_CLASS = 40

        def _spmm(row, col, val, x):
            msg = val[:, None] * x[col]
            return jax.ops.segment_sum(msg, row, num_segments=N_NODES)

        def _ngcf_layer(row, col, val, x, W1, W2):
            support = _spmm(row, col, val, x)
            return support @ W1 + support * x @ W2
        h1 = jax.nn.relu(_ngcf_layer(edge_row, edge_col, edge_val, emb, W1a, W2a))
        h2 = jax.nn.relu(_ngcf_layer(edge_row, edge_col, edge_val, emb, W1h, W2h))
        out = _ngcf_layer(edge_row, edge_col, edge_val, h2, W1o, W2o)
        return jax.nn.log_softmax(out, axis=1)
    y = _L0_rec_ref(r_x, L0_rec_edge_row, L0_rec_edge_col, L0_rec_edge_val, L0_rec_emb, L0_rec_W1a, L0_rec_W2a, L0_rec_W1h, L0_rec_W2h, L0_rec_W1o, L0_rec_W2o)
    return y

_drawn_inputs = setup_inputs


def setup_inputs(seed=0):
    import zlib

    import numpy as np

    out = dict(_drawn_inputs(seed))
    spreads = {}
    factors = {'L0_rec_edge_val': 4.305,
     'L0_rec_emb': 3.361,
     'L0_rec_W1h': 3.345,
     'L0_rec_W2h': 8.0,
     'L0_rec_W2o': 8.0}
    for name, (base, spread) in spreads.items():
        noise = np.random.default_rng([zlib.crc32(name.encode()), seed]).standard_normal(out[name].shape)
        drawn = base * np.exp(spread * noise) if base else spread * noise
        out[name] = jnp.asarray(drawn.astype(out[name].dtype))
    for name, factor in factors.items():
        out[name] = (out[name] * factor).astype(out[name].dtype)
    return out
```

```python
from contextlib import ExitStack

import concourse.bass as bass
from concourse import mybir

DT = mybir.dt
F32, F32R, I32, BF16, F16 = DT.float32, DT.float32r, DT.int32, DT.bfloat16, DT.float16
ALU = mybir.AluOpType
ACT = mybir.ActivationFunctionType
AXIS = mybir.AxisListType

P = 128
N_NODES, N_EDGES, D, N_CLASS = 2500, 40000, 1024, 40
M = 125
BINS = N_NODES // M
EP = 125
EJ = N_EDGES // EP
TILE = 128
PAIR = 2 * TILE
PAIRS = (N_EDGES + BINS * (PAIR - 1)) // PAIR
PAIRS += PAIRS % 2
TILES = 2 * PAIRS
RING = 4
KC = D // P
HALF = 512
N_FIELDS = 5
COL_MID = N_NODES // 2
STARTS, EXTRAS = 0, 32
MAX_PAIR = PAIRS - 1


def ngcf_kernel(nc, edge_row, edge_col, edge_val, emb, w1h, w2h, w1o, w2o, out):
    h2 = nc.dram_tensor("h2", (N_NODES, D), F32, kind="Internal").ap()
    sources = [emb, h2]
    source_blocks = [t.rearrange("(b p) d -> b p d", p=M) for t in sources]
    h2_blocks = source_blocks[1]

    with ExitStack() as ctx:
        def sb(name, shape, dt):
            return ctx.enter_context(nc.sbuf_tensor(name, shape, dt))

        def sem(name):
            return ctx.enter_context(nc.semaphore(name))

        w_hi = sb("w_hi", [P, 2 * KC, D], F32R)
        w_lo = sb("w_lo", [P, 2 * KC, D], F32R)
        raw = sb("raw", [P, RING, D], F32)
        msg_hi = sb("msg_hi", [P, RING, D], F32R)
        msg_lo = sb("msg_lo", [P, RING, D], F32R)
        row_hot = sb("row_hot", [P, 2, P], F32R)
        conv_hi = sb("conv_hi", [P, 2, 2, P], F32R)
        conv_lo = sb("conv_lo", [P, 2, 2, P], F32R)
        slots = sb("slots", [P, 3, TILES], F32)
        slot_val, slot_row, slot_col = slots[:, 0, :], slots[:, 1, :], slots[:, 2, :].bitcast(I32)
        hots_16 = slots[:, :, :].rearrange("p f t -> p (f t)").bitcast(F16)
        hot_hi = hots_16[:, 0:2 * TILES].rearrange("p (s t) -> p s t", s=2)
        hot_lo = hots_16[:, 2 * TILES:2 * TILES + 2 * N_FIELDS * P].rearrange(
            "p (s f l) -> p s f l", s=2, f=N_FIELDS)
        gather_idx = sb("gather_idx", [P, RING], I32)
        iota_row = sb("iota_row", [P, P], F32)
        iota_lo = sb("iota_lo", [P, P], F16)
        iota_hi = sb("iota_hi", [P, TILES], F16)
        ident = sb("ident", [P, P], F32)
        lower = sb("lower", [P, P], F32)
        ones = sb("ones", [P, P], F32)
        table = sb("table", [P, 64], I32)
        bin_stat = sb("bin_stat", [P, 8, BINS], F32)
        bin_int = sb("bin_int", [P, BINS], I32)
        stat = sb("stat", [P, 2, BINS], F32)
        region = sb("region", [P, 4608], F32)

        def edge_array(n):
            return region[0:EP, n * EJ:(n + 1) * EJ]

        e_row_i, e_col_i = edge_array(0).bitcast(I32), edge_array(1).bitcast(I32)
        e_pos_i, e_tmp_i = e_row_i, e_col_i
        e_val, e_rowf, e_bin = edge_array(2), edge_array(3), edge_array(4)
        e_rank = e_rowf
        fields = [edge_array(7), edge_array(8), edge_array(9), edge_array(5), edge_array(6)]
        v_hi, v_mid, v_lo, e_rloc, e_colc = fields
        e_ind, e_scan, e_tmp = edge_array(10), edge_array(11), edge_array(12)
        e_hi, e_lo = e_ind, e_scan
        e_half = region[0:EP, 12 * EJ:12 * EJ + EJ // 2].bitcast(BF16)

        support = region[0:M, 0:D]
        block = region[0:M, D:2 * D]
        h_out = region[0:M, 2 * D:3 * D]
        conv_f32 = region[:, 2 * D:2 * D + 512].rearrange("p (r s m) -> p r s m", r=2, s=2)
        w_out = region[:, 3 * D:3 * D + 2 * KC * N_CLASS].rearrange("p (w c k) -> p w c k", w=2, c=KC)
        LOG0 = 3 * D + 2 * KC * N_CLASS
        logits = region[0:M, LOG0:LOG0 + BINS * N_CLASS].rearrange("p (b k) -> p b k", b=BINS)
        exps = region[0:M, 0:BINS * N_CLASS].rearrange("p (b k) -> p b k", b=BINS)

        ps = ctx.enter_context(nc.psum_tensor("ps", [P, 8, HALF], F32))
        BASE_BANK, FIELD_BANK = 0, 1
        SUM_BANK, OUT_BANK, T_BANK = (0, 2), 4, 6

        edges_in, consts_ready, counts_ready, base_ready = (
            sem("edges_in"), sem("consts_ready"), sem("counts_ready"), sem("base_ready"))
        hot_ready, hot_used, slots_ready, table_ready = (
            sem("hot_ready"), sem("hot_used"), sem("slots_ready"), sem("table_ready"))
        w_in = [sem(f"w_in{s}") for s in range(RING)]
        w_hi_ready, w_lo_ready, w_out_in = sem("w_hi_ready"), sem("w_lo_ready"), sem("w_out_in")
        dve_step = sem("dve_step")
        LAYERS = (0, 1)

        def both(name):
            return [sem(f"{name}{layer}") for layer in LAYERS]

        row_in = [[sem(f"row_in{layer}_{s}") for s in range(RING)] for layer in LAYERS]
        idx_copied, pairs_asked, gathered = both("idx_copied"), both("pairs_asked"), both("gathered")
        msg_hi_ready, msg_lo_ready, row_hot_ready = both("msg_hi_ready"), both("msg_lo_ready"), both("row_hot_ready")
        slot_free = both("slot_free")
        block_in, support_ready, product_ready = both("block_in"), both("support_ready"), both("product_ready")
        turned, conv_hi_ready, conv_lo_ready = both("turned"), both("conv_hi_ready"), both("conv_lo_ready")
        chunk_done, out_ready = both("chunk_done"), both("out_ready")
        h2_stored = sem("h2_stored")
        soft_step, exp_ready, ln_ready, result_ready, stored = (
            sem("soft_step"), sem("exp_ready"), sem("ln_ready"), sem("result_ready"), sem("stored"))

        def bin_bounds(eng, b):
            first = eng.value_load(table[0:1, bass.ds(STARTS + b, 1)], min_val=0, max_val=MAX_PAIR)
            extra = eng.value_load(table[0:1, bass.ds(EXTRAS + b, 1)], min_val=0, max_val=MAX_PAIR)
            return first, extra

        def total_pairs(eng):
            return eng.value_load(table[0:1, STARTS + BINS:STARTS + BINS + 1], min_val=2, max_val=PAIRS)

        def portion(eng, first, extra, c, pair):
            lo = eng.snap(first + 1 + ((extra * c) >> 3))
            hi = eng.snap(first + 1 + ((extra * (c + 1)) >> 3))
            with eng.If(lo < hi):
                with eng.Fori(lo, hi) as i:
                    pair(i.with_bounds(min_val=1, max_val=MAX_PAIR))


        block_ctx = ctx.enter_context(nc.Block())

        @block_ctx.sync
        def _(sp):
            sp.dma_start(e_row_i, edge_row.rearrange("(p j) -> p j", p=EP)).then_inc(edges_in, 16)
            sp.dma_start(e_col_i, edge_col.rearrange("(p j) -> p j", p=EP)).then_inc(edges_in, 16)
            sp.dma_start(e_val, edge_val.rearrange("(p j) -> p j", p=EP)).then_inc(edges_in, 16)
            for q in range(2 * KC):
                if q >= RING:
                    sp.wait_ge(w_lo_ready, q - RING + 1)
                w = (w1h, w2h)[q // KC]
                c = q % KC
                sp.dma_start(raw[:, q % RING, :], w[c * P:(c + 1) * P, :]).then_inc(w_in[q % RING], 16)
            sp.wait_ge(slots_ready, 1)
            sp.dma_start(w_out[:, 0], w1o.rearrange("(c p) k -> p c k", p=P)).then_inc(w_out_in, 16)
            sp.dma_start(w_out[:, 1], w2o.rearrange("(c p) k -> p c k", p=P)).then_inc(w_out_in, 16)
            total = total_pairs(sp)
            for layer in LAYERS:
                with sp.Fori(0, total, 2) as i:
                    for s in range(RING):
                        sp.wait_ge(row_in[layer][s], i * 8 + 16)
                        sp.sem_inc(gathered[layer], 1)
            sp.wait_ge(result_ready, 1)
            sp.dma_start(out.rearrange("(b p) k -> p b k", p=M), logits).then_inc(stored, 16)
            sp.wait_ge(stored, 16)

        @block_ctx.gpsimd
        def _(pool):
            nc.gpsimd.iota(iota_row[:], pattern=[[1, P]], base=0, channel_multiplier=0,
                           allow_small_or_imprecise_dtypes=True).then_inc(consts_ready, 1)
            nc.gpsimd.iota(iota_lo[:], pattern=[[1, P]], base=0, channel_multiplier=0,
                           allow_small_or_imprecise_dtypes=True).then_inc(consts_ready, 1)
            nc.gpsimd.iota(iota_hi[:], pattern=[[1, TILES]], base=0, channel_multiplier=0,
                           allow_small_or_imprecise_dtypes=True).then_inc(consts_ready, 1)
            nc.gpsimd.memset(ones[:], 1.0).then_inc(consts_ready, 1)
            pool.wait_ge(consts_ready, 4)
            nc.gpsimd.affine_select(out=lower[:], in_=ones[:], compare_op=ALU.is_gt, fill=0.0, base=0,
                                    pattern=[[1, P]], channel_multiplier=-1).then_inc(consts_ready, 1)
            nc.gpsimd.affine_select(out=ident[:], in_=ones[:], compare_op=ALU.is_equal, fill=0.0, base=0,
                                    pattern=[[1, P]], channel_multiplier=-1).then_inc(consts_ready, 1)
            for q in range(2 * KC):
                pool.wait_ge(w_hi_ready, q + 1)
                nc.gpsimd.tensor_tensor(w_lo[:, q, :], raw[:, q % RING, :], w_hi[:, q, :].bitcast(F32),
                                        ALU.subtract).then_inc(w_lo_ready, 1)
            pool.wait_ge(slots_ready, 1)
            total = total_pairs(pool)
            for layer in LAYERS:
                if layer == 1:
                    pool.wait_ge(h2_stored, 16 * BINS)
                source = sources[layer]

                def gather_pair(i, h, free):
                    if free:
                        pool.wait_ge(msg_lo_ready[layer], i * 2 - 2)
                    nc.gpsimd.tensor_copy(gather_idx[:, 2 * h:2 * h + 2],
                                          slot_col[:, bass.ds(i * 2, 2)]).then_inc(idx_copied[layer], 1)
                    pool.wait_ge(idx_copied[layer], i + 1)
                    pool.sem_inc(pairs_asked[layer], 1)
                    for s in (2 * h, 2 * h + 1):
                        nc.gpsimd.indirect_dma_start(
                            out=raw[:, s, :], out_offset=None, in_=source,
                            in_offset=bass.IndirectOffsetOnAxis(ap=gather_idx[:, s:s + 1], axis=0),
                        ).then_inc(row_in[layer][s], 16)

                for h in range(2):
                    gather_pair(h, h, False)
                with pool.Fori(2, total, 2) as i:
                    i = i.with_bounds(min_val=2, max_val=PAIRS - 2)
                    for h in range(2):
                        gather_pair(i + h, h, True)

        @block_ctx.scalar
        def _(act):
            nc.scalar.preload_act_table_set("natural_log_exp_and_others")
            for q in range(2 * KC):
                act.wait_ge(w_in[q % RING], 16 * (q // RING + 1))
                nc.scalar.activation(w_hi[:, q, :], raw[:, q % RING, :], ACT.Copy).then_inc(w_hi_ready, 1)
            act.wait_ge(slots_ready, 1)
            for layer in LAYERS:
                def load_block(w):
                    act.dma_start(block, source_blocks[layer][bass.ds(w, 1)].rearrange("o p d -> (o p) d")
                                  ).then_inc(block_in[layer], 16)

                def pair(i):
                    slot = act.snap((i & 1) * 2)
                    for s in range(2):
                        act.wait_ge(gathered[layer], i * 2 + s + 1)
                        act.wait_ge(slot_free[layer], i * 2 + s + 1)
                        nc.scalar.activation(msg_hi[:, bass.ds(slot + s, 1), :].rearrange("p o d -> p (o d)"),
                                             raw[:, bass.ds(slot + s, 1), :].rearrange("p o d -> p (o d)"),
                                             ACT.Copy, scale=slot_val[:, bass.ds(i * 2 + s, 1)],
                                             ).then_inc(msg_hi_ready[layer], 1)

                def convert(w, c):
                    q = w * KC + c
                    act.wait_ge(turned[layer], q + 1)
                    if not isinstance(q, int) or q >= 2:
                        act.wait_ge(chunk_done[layer], q - 1)
                    turned_c = ps[:, T_BANK + c % 2, 0:2 * P].rearrange("p (s m) -> p s m", s=2)[:, :, 0:M]
                    to = (conv_hi, conv_f32)[layer][:, c % 2, :, 0:M]
                    nc.scalar.activation(to, turned_c, ACT.Copy).then_inc(conv_hi_ready[layer], 1)

                def finish(w):
                    act.wait_ge(chunk_done[layer], w * KC + KC)
                    if layer == 0:
                        if not isinstance(w, int) or w >= 1:
                            act.wait_ge(h2_stored, w * 16)
                        nc.scalar.activation(h_out, ps[0:M, OUT_BANK:OUT_BANK + 2, :].rearrange("p n d -> p (n d)"),
                                             ACT.Relu).then_inc(out_ready[layer], 1)
                    else:
                        nc.scalar.activation(logits[:, bass.ds(w, 1), :].rearrange("p o k -> p (o k)"),
                                             ps[0:M, OUT_BANK, 0:N_CLASS], ACT.Copy).then_inc(out_ready[layer], 1)

                def store(w):
                    if layer == 0:
                        act.wait_ge(out_ready[layer], w + 1)
                        act.dma_start(h2_blocks[bass.ds(w, 1)].rearrange("o p d -> (o p) d"), h_out
                                      ).then_inc(h2_stored, 16)

                def step(b, parity, sums=True, multiplies=True):
                    w = b - 1
                    later = not isinstance(b, int) or b >= 2
                    if sums:
                        first, extra = bin_bounds(act, b)
                        pair(first)
                    if multiplies:
                        end = first if sums else total_pairs(act)
                        act.wait_ge(slot_free[layer], end * 2 + RING)
                        if later:
                            act.wait_ge(turned[layer], w * KC)
                        nc.scalar.activation(
                            support, ps[0:M, SUM_BANK[1 - parity]:SUM_BANK[1 - parity] + 2, :].rearrange("p n d -> p (n d)"),
                            ACT.Copy).then_inc(support_ready[layer], 1)
                        convert(w, 0)
                        if later:
                            finish(w - 1)
                    for c in range(KC):
                        if sums:
                            portion(act, first, extra, c, pair)
                        if multiplies and c < KC - 1:
                            convert(w, c + 1)
                        if multiplies and c == 0 and later:
                            store(w - 1)
                    if multiplies and sums:
                        load_block(b)

                if layer == 1:
                    act.wait_ge(h2_stored, 16 * BINS)
                load_block(0)
                step(0, 0, multiplies=False)
                step(1, 1)
                with act.Fori(2, BINS, 2) as b:
                    b = b.with_bounds(min_val=2, max_val=BINS - 2)
                    step(b, 0)
                    step(b + 1, 1)
                step(BINS, 0, sums=False)
                finish(BINS - 1)
                store(BINS - 1)
            act.wait_ge(soft_step, 2)
            nc.scalar.activation(exps, logits, ACT.Exp).then_inc(exp_ready, 1)
            act.wait_ge(soft_step, 3)
            nc.scalar.activation(stat[0:M, 1, :], stat[0:M, 0, :], ACT.Ln).then_inc(ln_ready, 1)

        @block_ctx.vector
        def _(dve):
            steps = [0]

            def then(ins):
                steps[0] += 1
                ins.then_inc(dve_step, 1)
                dve.wait_ge(dve_step, steps[0])

            for layer in LAYERS:
                dve.sem_inc(slot_free[layer], RING)
            dve.wait_ge(edges_in, 48)
            rest = e_val
            for part in (v_hi, v_mid, v_lo):
                then(nc.vector.tensor_copy(e_half, rest))
                then(nc.vector.tensor_copy(part, e_half))
                if part is not v_lo:
                    then(nc.vector.tensor_tensor(e_val, rest, part, ALU.subtract))
            nc.vector.tensor_scalar(e_colc, e_col_i, -float(COL_MID), None, ALU.add)
            then(nc.vector.tensor_copy(e_rowf, e_row_i))
            then(nc.vector.tensor_scalar(e_bin, e_rowf, float(M), None, ALU.is_ge))
            for b in range(2, BINS):
                then(nc.vector.scalar_tensor_tensor(out=e_bin, in0=e_rowf, scalar=float(M * b), in1=e_bin,
                                                    op0=ALU.is_ge, op1=ALU.add))
            then(nc.vector.scalar_tensor_tensor(out=e_rloc, in0=e_bin, scalar=-float(M), in1=e_rowf,
                                                op0=ALU.mult, op1=ALU.add))
            then(nc.vector.memset(e_rank, 0.0))
            count = bin_stat[0:EP, 0, :]
            dve.wait_ge(consts_ready, 6)
            ones_row = ones[0:EP, 0:1].broadcast_to([EP, EJ])
            for b in range(BINS):
                then(nc.vector.tensor_scalar(e_ind, e_bin, float(b), None, ALU.is_equal))
                then(nc.vector.tensor_tensor_scan(e_scan, ones_row, e_ind, 0.0, ALU.mult, ALU.add))
                nc.vector.tensor_copy(count[:, b:b + 1], e_scan[:, EJ - 1:EJ])
                then(nc.vector.tensor_tensor(e_tmp, e_ind, e_scan, ALU.mult))
                then(nc.vector.tensor_tensor(e_rank, e_rank, e_tmp, ALU.add))
            nc.vector.tensor_copy(bin_stat[:, 7, 0:1], ones[:, 0:1]).then_inc(counts_ready, 1)
            dve.wait_ge(base_ready, 1)
            base = ps[0:EP, BASE_BANK, 0:BINS]
            totals = ps[:, BASE_BANK, 64:64 + BINS]
            pairs, incl, first, last = (bin_stat[:, k, :] for k in range(1, 5))
            off = bin_stat[0:EP, 5, :]
            then(nc.vector.tensor_scalar(bin_int[:], totals, float(PAIR - 1), None, ALU.add))
            then(nc.vector.tensor_scalar(bin_int[:], bin_int[:], 8, None, ALU.logical_shift_right))
            then(nc.vector.tensor_scalar(pairs, bin_int[:], 1.0, None, ALU.max))
            then(nc.vector.tensor_tensor_scan(incl, ones[:, 0:1].broadcast_to([P, BINS]), pairs, 0.0, ALU.mult, ALU.add))
            then(nc.vector.tensor_tensor(first, incl, pairs, ALU.subtract))
            then(nc.vector.tensor_scalar(bin_int[:, 0:1], incl[:, BINS - 1:BINS], 1.0, None, ALU.add))
            then(nc.vector.tensor_scalar(bin_int[:, 0:1], bin_int[:, 0:1], 1, 1, ALU.logical_shift_right, ALU.logical_shift_left))
            then(nc.vector.tensor_copy(incl[:, BINS - 1:BINS], bin_int[:, 0:1]))
            then(nc.vector.tensor_tensor(last, incl, first, ALU.subtract))
            nc.vector.tensor_copy(table[:, STARTS:STARTS + BINS], first)
            nc.vector.tensor_copy(table[:, STARTS + BINS:STARTS + BINS + 1], incl[:, BINS - 1:BINS])
            then(nc.vector.tensor_scalar(table[:, EXTRAS:EXTRAS + BINS], last, -1.0, None, ALU.add))
            then(nc.vector.scalar_tensor_tensor(out=off, in0=first[0:EP], scalar=float(PAIR), in1=base,
                                                op0=ALU.mult, op1=ALU.add))
            then(nc.vector.tensor_scalar(off, off, -1.0, None, ALU.add))
            for b in range(BINS):
                then(nc.vector.tensor_scalar(e_tmp, e_bin, float(b), off[:, b:b + 1], ALU.is_equal, ALU.mult))
                then(nc.vector.tensor_tensor(e_rank, e_rank, e_tmp, ALU.add))
            then(nc.vector.tensor_copy(e_pos_i, e_rank))
            then(nc.vector.tensor_scalar(e_tmp_i, e_pos_i, 7, None, ALU.logical_shift_right))
            then(nc.vector.tensor_copy(e_hi, e_tmp_i))
            then(nc.vector.tensor_scalar(e_tmp_i, e_pos_i, TILE - 1, None, ALU.bitwise_and))
            then(nc.vector.tensor_copy(e_lo, e_tmp_i))

            def hots(j, s, free):
                if free:
                    dve.wait_ge(hot_used, j - 1)
                nc.vector.tensor_scalar(hot_hi[0:EP, s, :], iota_hi[0:EP, :], e_hi[:, bass.ds(j, 1)], None, ALU.is_equal)
                for f in range(N_FIELDS):
                    to = hot_lo[0:EP, s, f, :]
                    last = nc.vector.tensor_scalar(to.bitcast(BF16) if f < 3 else to, iota_lo[0:EP, :],
                                                   e_lo[:, bass.ds(j, 1)], fields[f][:, bass.ds(j, 1)],
                                                   ALU.is_equal, ALU.mult)
                last.then_inc(hot_ready, 1)

            for j in range(4):
                hots(j, j % 2, j >= 2)
            with dve.Fori(4, EJ, 4) as j:
                j = j.with_bounds(min_val=4, max_val=EJ - 4)
                for u in range(4):
                    hots(j + u, u % 2, True)
            dve.wait_ge(hot_used, EJ)
            slot_field = [ps[:, FIELD_BANK + f, 0:TILES] for f in range(N_FIELDS)]
            then(nc.vector.tensor_copy(slot_val, slot_field[0]))
            then(nc.vector.tensor_tensor(slot_val, slot_val, slot_field[1], ALU.add))
            then(nc.vector.tensor_tensor(slot_val, slot_val, slot_field[2], ALU.add))
            then(nc.vector.tensor_copy(slot_row, slot_field[3]))
            nc.vector.tensor_scalar(slot_col, slot_field[4], float(COL_MID), None, ALU.add).then_inc(slots_ready, 1)

            for layer in LAYERS:
                def pair(i):
                    slot = dve.snap((i & 1) * 2)
                    for s in range(2):
                        dve.wait_ge(msg_hi_ready[layer], i * 2 + s + 1)
                        nc.vector.scalar_tensor_tensor(
                            out=msg_lo[:, bass.ds(slot + s, 1), :].rearrange("p o d -> p (o d)"),
                            in0=raw[:, bass.ds(slot + s, 1), :].rearrange("p o d -> p (o d)"),
                            scalar=slot_val[:, bass.ds(i * 2 + s, 1)],
                            in1=msg_hi[:, bass.ds(slot + s, 1), :].rearrange("p o d -> p (o d)").bitcast(F32),
                            op0=ALU.mult, op1=ALU.subtract).then_inc(msg_lo_ready[layer], 1)
                    for s in range(2):
                        dve.wait_ge(slot_free[layer], i * 2 + s + 3)
                        nc.vector.tensor_scalar(row_hot[:, s, :], iota_row[:], slot_row[:, bass.ds(i * 2 + s, 1)],
                                                None, ALU.is_equal).then_inc(row_hot_ready[layer], 1)

                def convert(w, c):
                    if layer == 0:
                        dve.wait_ge(conv_hi_ready[layer], w * KC + c + 1)
                        turned_c = ps[:, T_BANK + c % 2, 0:2 * P].rearrange("p (s m) -> p s m", s=2)[:, :, 0:M]
                        nc.vector.tensor_tensor(conv_lo[:, c % 2, :, 0:M], turned_c,
                                                conv_hi[:, c % 2, :, 0:M].bitcast(F32),
                                                ALU.subtract).then_inc(conv_lo_ready[layer], 1)

                def step(b, parity, sums=True, multiplies=True):
                    w = b - 1
                    if sums:
                        first, extra = bin_bounds(dve, b)
                        pair(first)
                    if multiplies:
                        dve.wait_ge(support_ready[layer], b)
                        dve.wait_ge(block_in[layer], b * 16)
                        nc.vector.tensor_tensor(block, support, block, ALU.mult).then_inc(product_ready[layer], 1)
                        convert(w, 0)
                    for c in range(KC):
                        if sums:
                            portion(dve, first, extra, c, pair)
                        if multiplies and c < KC - 1:
                            convert(w, c + 1)

                if layer == 0:
                    dve.wait_ge(dve_step, steps[0])
                    dve.wait_ge(slots_ready, 1)
                step(0, 0, multiplies=False)
                step(1, 1)
                with dve.Fori(2, BINS, 2) as b:
                    b = b.with_bounds(min_val=2, max_val=BINS - 2)
                    step(b, 0)
                    step(b + 1, 1)
                step(BINS, 0, sums=False)

            dve.wait_ge(out_ready[1], BINS)
            maxima = stat[0:M, 0, :]
            nc.vector.tensor_reduce(maxima, logits, AXIS.X, ALU.max).then_inc(soft_step, 1)
            dve.wait_ge(soft_step, 1)
            nc.vector.tensor_tensor(logits, logits, maxima.unsqueeze(2).broadcast_to([M, BINS, N_CLASS]),
                                    ALU.subtract).then_inc(soft_step, 1)
            dve.wait_ge(exp_ready, 1)
            nc.vector.tensor_reduce(maxima, exps, AXIS.X, ALU.add).then_inc(soft_step, 1)
            dve.wait_ge(ln_ready, 1)
            nc.vector.tensor_tensor(logits, logits, stat[0:M, 1, :].unsqueeze(2).broadcast_to([M, BINS, N_CLASS]),
                                    ALU.subtract).then_inc(result_ready, 1)

        @block_ctx.tensor
        def _(pe):
            pe.wait_ge(consts_ready, 6)
            pe.wait_ge(counts_ready, 1)
            nc.tensor.matmul(ps[0:EP, BASE_BANK, 0:BINS], lower[0:EP, 0:EP], bin_stat[0:EP, 0, :], start=True, stop=True)
            nc.tensor.matmul(ps[:, BASE_BANK, 64:64 + BINS], ones[0:EP, :], bin_stat[0:EP, 0, :],
                             start=True, stop=True).then_inc(base_ready, 1)

            def scatter(j, s, start):
                pe.wait_ge(hot_ready, j + 1)
                for f in range(N_FIELDS):
                    hot = hot_lo[0:EP, s, f, :]
                    last = nc.tensor.matmul(ps[:, FIELD_BANK + f, 0:TILES], hot.bitcast(BF16) if f < 3 else hot,
                                            hot_hi[0:EP, s, :], start=start, stop=True, skip_group_check=True)
                last.then_inc(hot_used, 1)

            for j in range(4):
                scatter(j, j % 2, j == 0)
            with pe.Fori(4, EJ, 4) as j:
                for u in range(4):
                    scatter(j + u, u % 2, False)

            pe.wait_ge(slots_ready, 1)
            for layer in LAYERS:
                def pair(i, parity, start):
                    slot = pe.snap((i & 1) * 2)
                    for s in range(2):
                        pe.wait_ge(msg_lo_ready[layer], i * 2 + s + 1)
                        pe.wait_ge(row_hot_ready[layer], i * 2 + s + 1)
                        for part in (msg_hi, msg_lo):
                            for n in range(2):
                                last = nc.tensor.matmul(
                                    ps[:, SUM_BANK[parity] + n, :], row_hot[:, s, :],
                                    part[:, bass.ds(slot + s, 1), n * HALF:(n + 1) * HALF].rearrange("p o d -> p (o d)"),
                                    start=start and s == 0 and part is msg_hi, stop=True, skip_group_check=True)
                        last.then_inc(slot_free[layer], 1)

                def turn(w, c):
                    q = w * KC + c
                    if not isinstance(q, int) or q >= 2:
                        pe.wait_ge((conv_lo_ready, conv_hi_ready)[layer][layer], q - 1)
                    for k, rows in enumerate((support, block)):
                        last = nc.tensor.transpose(ps[:, T_BANK + c % 2, k * P:k * P + M],
                                                   rows[:, c * P:(c + 1) * P], ident[0:M, 0:M])
                    last.then_inc(turned[layer], 1)

                def chunk(w, c):
                    q = w * KC + c
                    pe.wait_ge((conv_lo_ready, conv_hi_ready)[layer][layer], q + 1)
                    if c == 0 and (not isinstance(w, int) or w >= 1):
                        pe.wait_ge(out_ready[layer], w)
                    for k in range(2):
                        if layer == 0:
                            hi, lo = conv_hi[:, c % 2, k, 0:M], conv_lo[:, c % 2, k, 0:M]
                            for x, y in ((hi, w_hi), (hi, w_lo), (lo, w_hi)):
                                for n in range(2):
                                    last = nc.tensor.matmul(
                                        ps[0:M, OUT_BANK + n, :], x, y[:, k * KC + c, n * HALF:(n + 1) * HALF],
                                        start=c == 0 and k == 0 and x is hi and y is w_hi, stop=True, skip_group_check=True)
                        else:
                            last = nc.tensor.matmul(ps[0:M, OUT_BANK, 0:N_CLASS], conv_f32[:, c % 2, k, 0:M],
                                                    w_out[:, k, c, :], start=c == 0 and k == 0, stop=True,
                                                    skip_group_check=True)
                    last.then_inc(chunk_done[layer], 1)

                def step(b, parity, sums=True, multiplies=True):
                    w = b - 1
                    if sums:
                        first, extra = bin_bounds(pe, b)
                        if not isinstance(b, int) or b >= 2:
                            pe.wait_ge(support_ready[layer], b - 1)
                        pair(first, parity, True)
                    if multiplies:
                        pe.wait_ge(support_ready[layer], b)
                        pe.wait_ge(product_ready[layer], b)
                        turn(w, 0)
                    for c in range(KC):
                        if sums:
                            portion(pe, first, extra, c, lambda i: pair(i, parity, False))
                        if multiplies:
                            if c < KC - 1:
                                turn(w, c + 1)
                            chunk(w, c)

                if layer == 0:
                    pe.wait_ge(w_lo_ready, 2 * KC)
                else:
                    pe.wait_ge(w_out_in, 32)
                step(0, 0, multiplies=False)
                step(1, 1)
                with pe.Fori(2, BINS, 2) as b:
                    b = b.with_bounds(min_val=2, max_val=BINS - 2)
                    step(b, 0)
                    step(b + 1, 1)
                step(BINS, 0, sums=False)


_INS = ["L0_rec_edge_row", "L0_rec_edge_col", "L0_rec_edge_val", "L0_rec_emb",
        "L0_rec_W1h", "L0_rec_W2h", "L0_rec_W1o", "L0_rec_W2o"]


def kernel(**inputs):
    import numpy as np
    import concourse.bacc as bacc
    from concourse.bass_utils import run_bass_kernel_spmd

    nc = bacc.Bacc("TRN2", target_bir_lowering=False, num_devices=1)
    arrays, args = {}, []
    for name in _INS:
        a = np.ascontiguousarray(inputs[name])
        arrays[f"in_{name}"] = a
        args.append(nc.dram_tensor(f"in_{name}", a.shape, mybir.dt.from_np(a.dtype), kind="ExternalInput").ap())
    out = nc.dram_tensor("out", (N_NODES, N_CLASS), F32, kind="ExternalOutput").ap()
    ngcf_kernel(nc, *args, out)
    return run_bass_kernel_spmd(nc, [arrays], core_ids=[0]).results[0]["out"]
```

```python
from contextlib import ExitStack

import concourse.bass as bass
from concourse import mybir

DT = mybir.dt
F32, F32R, I32, BF16, F16 = DT.float32, DT.float32r, DT.int32, DT.bfloat16, DT.float16
ALU = mybir.AluOpType
ACT = mybir.ActivationFunctionType
AXIS = mybir.AxisListType

P = 128
N_NODES, N_EDGES, D, N_CLASS = 2500, 40000, 1024, 40
M = 125
BINS = N_NODES // M
EP = 125
EJ = N_EDGES // EP
TILE = 128
PAIR = 2 * TILE
PAIRS = (N_EDGES + BINS * (PAIR - 1)) // PAIR
PAIRS += PAIRS % 2
TILES = 2 * PAIRS
RING = 4
KC = D // P
HALF = 512
N_FIELDS = 5
GROUP = 8
COL_MID = N_NODES // 2
UNITS = (KC, KC // 2)
TURN = ({0: [0, 1], 1: [2], 2: [3], 3: [4], 4: [5], 5: [6], 6: [7]}, {0: [0, 1], 3: [2], 4: [3]})
CONVERT = ({0: [0, 1], 2: [2], 3: [3], 4: [4], 5: [5], 6: [6], 7: [7]}, {2: [0], 3: [1], 6: [2], 7: [3]})
MULTIPLY = ({1: [0], 2: [1], 3: [2], 4: [3], 5: [4], 6: [5], 7: [6, 7]}, {4: [0], 5: [1], 7: [2, 3]})
STARTS, EXTRAS = 0, 32
MAX_PAIR = PAIRS - 1


def ngcf_kernel(nc, edge_row, edge_col, edge_val, emb, w1h, w2h, w1o, w2o, out):
    h2 = nc.dram_tensor("h2", (N_NODES, D), F32, kind="Internal").ap()
    sources = [emb, h2]
    source_blocks = [t.rearrange("(b p) d -> b p d", p=M) for t in sources]
    h2_blocks = source_blocks[1]

    with ExitStack() as ctx:
        def sb(name, shape, dt):
            return ctx.enter_context(nc.sbuf_tensor(name, shape, dt))

        def sem(name):
            return ctx.enter_context(nc.semaphore(name))

        w_hi = sb("w_hi", [P, 2 * KC, D], F32R)
        w_lo = sb("w_lo", [P, 2 * KC, D], F32R)
        raw = sb("raw", [P, RING, D], F32)
        slot_val = sb("slot_val", [P, TILES], F32)
        slot_row = sb("slot_row", [P, TILES], F32)
        slot_col = sb("slot_col", [P, TILES], I32)
        gather_idx = sb("gather_idx", [P, RING], I32)
        iota_row = sb("iota_row", [P, P], F32)
        ident = sb("ident", [P, P], F32)
        table = sb("table", [P, 64], I32)

        with ExitStack() as binning:
            def bin_sb(name, shape, dt):
                return binning.enter_context(nc.sbuf_tensor(name, shape, dt))

            edge = bin_sb("edge", [P, 8, EJ], F32)
            edge_16 = bin_sb("edge_16", [P, N_FIELDS + 1, EJ], F16)
            hot_hi = bin_sb("hot_hi", [P, 2, GROUP, TILES], F16)
            hot_place = bin_sb("hot_place", [P, P, GROUP], F16)
            hot_lo = bin_sb("hot_lo", [P, 2, N_FIELDS, P, GROUP], F16)
            iota_place = bin_sb("iota_place", [P, P, GROUP], F16)
            iota_hi = bin_sb("iota_hi", [P, TILES], F16)
            lower = bin_sb("lower", [P, P], F32)
            ones = bin_sb("ones", [P, P], F32)
            bin_stat = bin_sb("bin_stat", [P, 6, BINS], F32)
            bin_int = bin_sb("bin_int", [P, BINS], I32)

        e_row_i, e_col_i = edge[0:EP, 0].bitcast(I32), edge[0:EP, 1].bitcast(I32)
        e_pos_i, e_tmp_i = e_row_i, e_col_i
        e_val, e_rowf, e_bin, e_ind, e_scan, e_tmp = (edge[0:EP, n] for n in range(2, 8))
        e_rank, e_hi = e_rowf, e_ind
        fields_bf, fields_f16 = edge_16[0:EP, 0:3].bitcast(BF16), edge_16[0:EP, 3:5]
        e_rloc, e_colc, e_lo = (edge_16[0:EP, n] for n in range(3, 6))

        msg_hi = sb("msg_hi", [P, RING, D], F32R)
        msg_lo = sb("msg_lo", [P, RING, D], F32R)
        row_hot = sb("row_hot", [P, 2, P], F32R)
        conv_hi = sb("conv_hi", [P, 2, 2, P], F32R)
        conv_lo = sb("conv_lo", [P, 2, 2, P], F32R)
        support_sb = sb("support", [P, D], F32)
        block_sb = sb("own_rows", [P, D], F32)
        h_sb = sb("h_sb", [P, D], F32)
        w_out = sb("w_out", [P, 2, KC, N_CLASS], F32)
        logits_sb = sb("logits", [P, BINS, N_CLASS], F32)
        stat = sb("stat", [P, 2, BINS], F32)
        support, block, h_out = support_sb[0:M], block_sb[0:M], h_sb[0:M]
        conv_f32 = h_sb[:, :].rearrange("p (r s m) -> p r s m", r=2, s=4)
        logits = logits_sb[0:M]
        exps = support_sb[0:M, 0:BINS * N_CLASS].rearrange("p (b k) -> p b k", b=BINS)

        ps = ctx.enter_context(nc.psum_tensor("ps", [P, 8, HALF], F32))
        BASE_BANK, FIELD_BANK = 0, 1
        SUM_BANK, OUT_BANK, T_BANK = (0, 2), 4, 6

        edges_in, consts_ready, counts_ready, base_ready = (
            sem("edges_in"), sem("consts_ready"), sem("counts_ready"), sem("base_ready"))
        place_ready, hot_ready, hot_used, slots_ready = (
            sem("place_ready"), sem("hot_ready"), sem("hot_used"), sem("slots_ready"))
        w_in = [sem(f"w_in{s}") for s in range(RING)]
        w_hi_ready, w_lo_ready, w_out_in = sem("w_hi_ready"), sem("w_lo_ready"), sem("w_out_in")
        dve_step = sem("dve_step")
        LAYERS = (0, 1)

        def both(name):
            return [sem(f"{name}{layer}") for layer in LAYERS]

        row_in = [[sem(f"row_in{layer}_{s}") for s in range(RING)] for layer in LAYERS]
        idx_copied, pairs_asked, gathered = both("idx_copied"), both("pairs_asked"), both("gathered")
        msg_hi_ready, msg_lo_ready, row_hot_ready = both("msg_hi_ready"), both("msg_lo_ready"), both("row_hot_ready")
        slot_free = both("slot_free")
        block_in, support_ready, product_ready = both("block_in"), both("support_ready"), both("product_ready")
        turned, conv_hi_ready, conv_lo_ready = both("turned"), both("conv_hi_ready"), sem("conv_lo_ready")
        unit_done, out_ready = both("unit_done"), both("out_ready")
        h2_stored = sem("h2_stored")
        soft_step, exp_ready, ln_ready, result_ready, stored = (
            sem("soft_step"), sem("exp_ready"), sem("ln_ready"), sem("result_ready"), sem("stored"))

        def bin_bounds(eng, b):
            first = eng.value_load(table[0:1, bass.ds(STARTS + b, 1)], min_val=0, max_val=MAX_PAIR)
            extra = eng.value_load(table[0:1, bass.ds(EXTRAS + b, 1)], min_val=0, max_val=MAX_PAIR)
            return first, extra

        def total_pairs(eng):
            return eng.value_load(table[0:1, STARTS + BINS:STARTS + BINS + 1], min_val=2, max_val=PAIRS)

        def portion(eng, first, extra, c, pair):
            lo = eng.snap(first + 1 + ((extra * c + KC - 1) >> 3))
            hi = eng.snap(first + 1 + ((extra * (c + 1) + KC - 1) >> 3))
            with eng.If(lo < hi):
                with eng.Fori(lo, hi) as i:
                    pair(i.with_bounds(min_val=1, max_val=MAX_PAIR))


        def unit_chunks(layer, u):
            size = KC // UNITS[layer]
            return range(u * size, (u + 1) * size)

        def turned_unit(layer, u):
            n = 2 * KC // UNITS[layer]
            return ps[:, T_BANK + u % 2, 0:n * P].rearrange("p (s m) -> p s m", s=n)[:, :, 0:M]

        block_ctx = ctx.enter_context(nc.Block())

        @block_ctx.sync
        def _(sp):
            sp.dma_start(e_row_i, edge_row.rearrange("(p j) -> p j", p=EP)).then_inc(edges_in, 16)
            sp.dma_start(e_col_i, edge_col.rearrange("(p j) -> p j", p=EP)).then_inc(edges_in, 16)
            sp.dma_start(e_val, edge_val.rearrange("(p j) -> p j", p=EP)).then_inc(edges_in, 16)
            for q in range(2 * KC):
                if q >= RING:
                    sp.wait_ge(w_lo_ready, q - RING + 1)
                w = (w1h, w2h)[q // KC]
                c = q % KC
                sp.dma_start(raw[:, q % RING, :], w[c * P:(c + 1) * P, :]).then_inc(w_in[q % RING], 16)
            sp.wait_ge(slots_ready, 1)
            sp.dma_start(w_out[:, 0], w1o.rearrange("(c p) k -> p c k", p=P)).then_inc(w_out_in, 16)
            sp.dma_start(w_out[:, 1], w2o.rearrange("(c p) k -> p c k", p=P)).then_inc(w_out_in, 16)
            total = total_pairs(sp)
            for layer in LAYERS:
                with sp.Fori(0, total, 2) as i:
                    for s in range(RING):
                        sp.wait_ge(row_in[layer][s], i * 8 + 16)
                        sp.sem_inc(gathered[layer], 1)
            sp.wait_ge(result_ready, 1)
            sp.dma_start(out.rearrange("(b p) k -> p b k", p=M), logits).then_inc(stored, 16)
            sp.wait_ge(stored, 16)

        @block_ctx.gpsimd
        def _(pool):
            nc.gpsimd.iota(iota_row[:], pattern=[[1, P]], base=0, channel_multiplier=0,
                           allow_small_or_imprecise_dtypes=True).then_inc(consts_ready, 1)
            nc.gpsimd.iota(iota_place[:], pattern=[[1, P], [0, GROUP]], base=0, channel_multiplier=0,
                           allow_small_or_imprecise_dtypes=True).then_inc(consts_ready, 1)
            nc.gpsimd.iota(iota_hi[:], pattern=[[1, TILES]], base=0, channel_multiplier=0,
                           allow_small_or_imprecise_dtypes=True).then_inc(consts_ready, 1)
            nc.gpsimd.memset(ones[:], 1.0).then_inc(consts_ready, 1)
            pool.wait_ge(consts_ready, 4)
            nc.gpsimd.affine_select(out=lower[:], in_=ones[:], compare_op=ALU.is_gt, fill=0.0, base=0,
                                    pattern=[[1, P]], channel_multiplier=-1).then_inc(consts_ready, 1)
            nc.gpsimd.affine_select(out=ident[:], in_=ones[:], compare_op=ALU.is_equal, fill=0.0, base=0,
                                    pattern=[[1, P]], channel_multiplier=-1).then_inc(consts_ready, 1)
            for q in range(2 * KC):
                pool.wait_ge(w_hi_ready, q + 1)
                nc.gpsimd.tensor_tensor(w_lo[:, q, :], raw[:, q % RING, :], w_hi[:, q, :].bitcast(F32),
                                        ALU.subtract).then_inc(w_lo_ready, 1)
            pool.wait_ge(slots_ready, 1)
            total = total_pairs(pool)
            for layer in LAYERS:
                if layer == 1:
                    pool.wait_ge(h2_stored, 16 * BINS)
                source = sources[layer]

                def gather_pair(i, h, free):
                    if free:
                        pool.wait_ge(msg_lo_ready[layer], i * 2 - 2)
                    nc.gpsimd.tensor_copy(gather_idx[:, 2 * h:2 * h + 2],
                                          slot_col[:, bass.ds(i * 2, 2)]).then_inc(idx_copied[layer], 1)
                    pool.wait_ge(idx_copied[layer], i + 1)
                    pool.sem_inc(pairs_asked[layer], 1)
                    for s in (2 * h, 2 * h + 1):
                        nc.gpsimd.indirect_dma_start(
                            out=raw[:, s, :], out_offset=None, in_=source,
                            in_offset=bass.IndirectOffsetOnAxis(ap=gather_idx[:, s:s + 1], axis=0),
                        ).then_inc(row_in[layer][s], 16)

                for h in range(2):
                    gather_pair(h, h, False)
                with pool.Fori(2, total, 2) as i:
                    i = i.with_bounds(min_val=2, max_val=PAIRS - 2)
                    for h in range(2):
                        gather_pair(i + h, h, True)

        @block_ctx.scalar
        def _(act):
            nc.scalar.preload_act_table_set("natural_log_exp_and_others")
            for q in range(2 * KC):
                act.wait_ge(w_in[q % RING], 16 * (q // RING + 1))
                nc.scalar.activation(w_hi[:, q, :], raw[:, q % RING, :], ACT.Copy).then_inc(w_hi_ready, 1)
            act.wait_ge(slots_ready, 1)
            for layer in LAYERS:
                def load_block(w):
                    act.dma_start(block, source_blocks[layer][bass.ds(w, 1)].rearrange("o p d -> (o p) d")
                                  ).then_inc(block_in[layer], 16)

                def pair(i):
                    slot = act.snap((i & 1) * 2)
                    for s in range(2):
                        act.wait_ge(gathered[layer], i * 2 + s + 1)
                        act.wait_ge(slot_free[layer], i * 2 + s + 1)
                        nc.scalar.activation(msg_hi[:, bass.ds(slot + s, 1), :].rearrange("p o d -> p (o d)"),
                                             raw[:, bass.ds(slot + s, 1), :].rearrange("p o d -> p (o d)"),
                                             ACT.Copy, scale=slot_val[:, bass.ds(i * 2 + s, 1)],
                                             ).then_inc(msg_hi_ready[layer], 1)

                def convert(w, u):
                    q = w * UNITS[layer] + u
                    act.wait_ge(turned[layer], q + 1)
                    if not isinstance(q, int) or q >= 2:
                        act.wait_ge(unit_done[layer], q - 1)
                    nc.scalar.activation((conv_hi, conv_f32)[layer][:, u % 2, :, 0:M], turned_unit(layer, u),
                                         ACT.Copy).then_inc(conv_hi_ready[layer], 1)

                def finish(w):
                    act.wait_ge(unit_done[layer], (w + 1) * UNITS[layer])
                    if layer == 0:
                        if not isinstance(w, int) or w >= 1:
                            act.wait_ge(h2_stored, w * 16)
                        nc.scalar.activation(h_out, ps[0:M, OUT_BANK:OUT_BANK + 2, :].rearrange("p n d -> p (n d)"),
                                             ACT.Relu).then_inc(out_ready[layer], 1)
                    else:
                        nc.scalar.activation(logits[:, bass.ds(w, 1), :].rearrange("p o k -> p (o k)"),
                                             ps[0:M, OUT_BANK, 0:N_CLASS], ACT.Copy).then_inc(out_ready[layer], 1)

                def store(w):
                    if layer == 0:
                        act.wait_ge(out_ready[layer], w + 1)
                        act.dma_start(h2_blocks[bass.ds(w, 1)].rearrange("o p d -> (o p) d"), h_out
                                      ).then_inc(h2_stored, 16)

                def leave(b, parity, end, later):
                    act.wait_ge(slot_free[layer], end * 2 + RING)
                    if later:
                        act.wait_ge(turned[layer], (b - 1) * UNITS[layer])
                    nc.scalar.activation(
                        support, ps[0:M, SUM_BANK[1 - parity]:SUM_BANK[1 - parity] + 2, :].rearrange("p n d -> p (n d)"),
                        ACT.Copy).then_inc(support_ready[layer], 1)

                def step(b, parity, sums=True, multiplies=True):
                    w = b - 1
                    later = not isinstance(b, int) or b >= 2
                    if sums:
                        first, extra = bin_bounds(act, b)
                        pair(first)
                    end = first if sums else total_pairs(act)
                    for c in range(KC):
                        if sums:
                            portion(act, first, extra, c, pair)
                        if multiplies:
                            if c == 0:
                                leave(b, parity, end, later)
                            for u in CONVERT[layer].get(c, []):
                                convert(w, u)
                            if c == 0 and later:
                                finish(w - 1)
                            if c == 1 and later:
                                store(w - 1)
                    if multiplies and sums:
                        load_block(b)

                if layer == 1:
                    act.wait_ge(h2_stored, 16 * BINS)
                load_block(0)
                step(0, 0, multiplies=False)
                step(1, 1)
                with act.Fori(2, BINS, 2) as b:
                    b = b.with_bounds(min_val=2, max_val=BINS - 2)
                    step(b, 0)
                    step(b + 1, 1)
                step(BINS, 0, sums=False)
                finish(BINS - 1)
                store(BINS - 1)
            act.wait_ge(soft_step, 2)
            nc.scalar.activation(exps, logits, ACT.Exp).then_inc(exp_ready, 1)
            act.wait_ge(soft_step, 3)
            nc.scalar.activation(stat[0:M, 1, :], stat[0:M, 0, :], ACT.Ln).then_inc(ln_ready, 1)

        @block_ctx.vector
        def _(dve):
            steps = [0]

            def then(ins):
                steps[0] += 1
                ins.then_inc(dve_step, 1)
                dve.wait_ge(dve_step, steps[0])

            for layer in LAYERS:
                dve.sem_inc(slot_free[layer], RING)
            dve.wait_ge(edges_in, 48)
            for k in range(3):
                then(nc.vector.tensor_copy(fields_bf[:, k], e_val))
                if k < 2:
                    then(nc.vector.tensor_tensor(e_val, e_val, fields_bf[:, k], ALU.subtract))
            nc.vector.tensor_scalar(e_colc, e_col_i, -float(COL_MID), None, ALU.add)
            then(nc.vector.tensor_copy(e_rowf, e_row_i))
            then(nc.vector.tensor_scalar(e_bin, e_rowf, float(M), None, ALU.is_ge))
            for b in range(2, BINS):
                then(nc.vector.scalar_tensor_tensor(out=e_bin, in0=e_rowf, scalar=float(M * b), in1=e_bin,
                                                    op0=ALU.is_ge, op1=ALU.add))
            then(nc.vector.scalar_tensor_tensor(out=e_rloc, in0=e_bin, scalar=-float(M), in1=e_rowf,
                                                op0=ALU.mult, op1=ALU.add))
            then(nc.vector.memset(e_rank, 0.0))
            count = bin_stat[0:EP, 0, :]
            dve.wait_ge(consts_ready, 6)
            ones_row = ones[0:EP, 0:1].broadcast_to([EP, EJ])
            for b in range(BINS):
                then(nc.vector.tensor_scalar(e_ind, e_bin, float(b), None, ALU.is_equal))
                then(nc.vector.tensor_tensor_scan(e_scan, ones_row, e_ind, 0.0, ALU.mult, ALU.add))
                nc.vector.tensor_copy(count[:, b:b + 1], e_scan[:, EJ - 1:EJ])
                then(nc.vector.tensor_tensor(e_tmp, e_ind, e_scan, ALU.mult))
                then(nc.vector.tensor_tensor(e_rank, e_rank, e_tmp, ALU.add))
            dve.sem_inc(counts_ready, 1)
            dve.wait_ge(base_ready, 1)
            base = ps[0:EP, BASE_BANK, 0:BINS]
            totals = ps[:, BASE_BANK, 64:64 + BINS]
            pairs, incl, first, last = (bin_stat[:, k, :] for k in range(1, 5))
            off = bin_stat[0:EP, 5, :]
            then(nc.vector.tensor_scalar(bin_int[:], totals, float(PAIR - 1), None, ALU.add))
            then(nc.vector.tensor_scalar(bin_int[:], bin_int[:], 8, None, ALU.logical_shift_right))
            then(nc.vector.tensor_scalar(pairs, bin_int[:], 1.0, None, ALU.max))
            then(nc.vector.tensor_tensor_scan(incl, ones[:, 0:1].broadcast_to([P, BINS]), pairs, 0.0, ALU.mult, ALU.add))
            then(nc.vector.tensor_tensor(first, incl, pairs, ALU.subtract))
            then(nc.vector.tensor_scalar(bin_int[:, 0:1], incl[:, BINS - 1:BINS], 1.0, None, ALU.add))
            then(nc.vector.tensor_scalar(bin_int[:, 0:1], bin_int[:, 0:1], 1, 1, ALU.logical_shift_right, ALU.logical_shift_left))
            then(nc.vector.tensor_copy(incl[:, BINS - 1:BINS], bin_int[:, 0:1]))
            then(nc.vector.tensor_tensor(last, incl, first, ALU.subtract))
            nc.vector.tensor_copy(table[:, STARTS:STARTS + BINS], first)
            nc.vector.tensor_copy(table[:, STARTS + BINS:STARTS + BINS + 1], incl[:, BINS - 1:BINS])
            then(nc.vector.tensor_scalar(table[:, EXTRAS:EXTRAS + BINS], last, -1.0, None, ALU.add))
            then(nc.vector.scalar_tensor_tensor(out=off, in0=first[0:EP], scalar=float(PAIR), in1=base,
                                                op0=ALU.mult, op1=ALU.add))
            then(nc.vector.tensor_scalar(off, off, -1.0, None, ALU.add))
            for b in range(BINS):
                then(nc.vector.tensor_scalar(e_tmp, e_bin, float(b), off[:, b:b + 1], ALU.is_equal, ALU.mult))
                then(nc.vector.tensor_tensor(e_rank, e_rank, e_tmp, ALU.add))
            then(nc.vector.tensor_copy(e_pos_i, e_rank))
            then(nc.vector.tensor_scalar(e_tmp_i, e_pos_i, 7, None, ALU.logical_shift_right))
            then(nc.vector.tensor_copy(e_hi, e_tmp_i))
            then(nc.vector.tensor_scalar(e_tmp_i, e_pos_i, TILE - 1, None, ALU.bitwise_and))
            then(nc.vector.tensor_copy(e_lo, e_tmp_i))

            def hots(g, s, free):
                if free:
                    dve.wait_ge(hot_used, g - 1)
                if not isinstance(g, int) or g >= 1:
                    dve.wait_ge(hot_ready, g)
                columns = bass.ds(g * GROUP, GROUP)

                def by_place(values):
                    return values.unsqueeze(1).broadcast_to([EP, P, GROUP])

                nc.vector.tensor_tensor(hot_place[0:EP], iota_place[0:EP], by_place(e_lo[:, columns]),
                                        ALU.is_equal).then_inc(place_ready, 1)
                for u in range(GROUP):
                    nc.vector.tensor_scalar(hot_hi[0:EP, s, u, :], iota_hi[0:EP, :], e_hi[:, bass.ds(g * GROUP + u, 1)],
                                            None, ALU.is_equal)
                dve.wait_ge(place_ready, g + 1)
                for f in range(N_FIELDS):
                    to = hot_lo[0:EP, s, f]
                    last = nc.vector.tensor_tensor(
                        to.bitcast(BF16) if f < 3 else to, hot_place[0:EP],
                        by_place((fields_bf[:, f] if f < 3 else fields_f16[:, f - 3])[:, columns]), ALU.mult)
                last.then_inc(hot_ready, 1)

            for g in range(2):
                hots(g, g % 2, False)
            with dve.Fori(2, EJ // GROUP, 2) as g:
                g = g.with_bounds(min_val=2, max_val=EJ // GROUP - 2)
                for u in range(2):
                    hots(g + u, u, True)
            dve.wait_ge(hot_used, EJ // GROUP)
            slot_field = [ps[:, FIELD_BANK + f, 0:TILES] for f in range(N_FIELDS)]
            then(nc.vector.tensor_copy(slot_val[:], slot_field[0]))
            then(nc.vector.tensor_tensor(slot_val[:], slot_val[:], slot_field[1], ALU.add))
            then(nc.vector.tensor_tensor(slot_val[:], slot_val[:], slot_field[2], ALU.add))
            then(nc.vector.tensor_copy(slot_row[:], slot_field[3]))
            nc.vector.tensor_scalar(slot_col[:], slot_field[4], float(COL_MID), None, ALU.add).then_inc(slots_ready, 1)

            for layer in LAYERS:
                def pair(i):
                    slot = dve.snap((i & 1) * 2)
                    for s in range(2):
                        dve.wait_ge(msg_hi_ready[layer], i * 2 + s + 1)
                        nc.vector.scalar_tensor_tensor(
                            out=msg_lo[:, bass.ds(slot + s, 1), :].rearrange("p o d -> p (o d)"),
                            in0=raw[:, bass.ds(slot + s, 1), :].rearrange("p o d -> p (o d)"),
                            scalar=slot_val[:, bass.ds(i * 2 + s, 1)],
                            in1=msg_hi[:, bass.ds(slot + s, 1), :].rearrange("p o d -> p (o d)").bitcast(F32),
                            op0=ALU.mult, op1=ALU.subtract).then_inc(msg_lo_ready[layer], 1)
                    for s in range(2):
                        dve.wait_ge(slot_free[layer], i * 2 + s + 3)
                        nc.vector.tensor_scalar(row_hot[:, s, :], iota_row[:], slot_row[:, bass.ds(i * 2 + s, 1)],
                                                None, ALU.is_equal).then_inc(row_hot_ready[layer], 1)

                def convert(w, u):
                    dve.wait_ge(conv_hi_ready[layer], w * UNITS[layer] + u + 1)
                    nc.vector.tensor_tensor(conv_lo[:, u % 2, :, 0:M], turned_unit(layer, u),
                                            conv_hi[:, u % 2, :, 0:M].bitcast(F32),
                                            ALU.subtract).then_inc(conv_lo_ready, 1)

                def step(b, parity, sums=True, multiplies=True):
                    if sums:
                        first, extra = bin_bounds(dve, b)
                        pair(first)
                    for c in range(KC):
                        if sums:
                            portion(dve, first, extra, c, pair)
                        if multiplies:
                            if c == 0:
                                dve.wait_ge(support_ready[layer], b)
                                dve.wait_ge(block_in[layer], b * 16)
                                nc.vector.tensor_tensor(block, support, block, ALU.mult
                                                        ).then_inc(product_ready[layer], 1)
                            if layer == 0:
                                for u in CONVERT[layer].get(c, []):
                                    convert(b - 1, u)

                if layer == 0:
                    dve.wait_ge(dve_step, steps[0])
                    dve.wait_ge(slots_ready, 1)
                step(0, 0, multiplies=False)
                step(1, 1)
                with dve.Fori(2, BINS, 2) as b:
                    b = b.with_bounds(min_val=2, max_val=BINS - 2)
                    step(b, 0)
                    step(b + 1, 1)
                step(BINS, 0, sums=False)

            dve.wait_ge(out_ready[1], BINS)
            maxima = stat[0:M, 0, :]
            nc.vector.tensor_reduce(maxima, logits, AXIS.X, ALU.max).then_inc(soft_step, 1)
            dve.wait_ge(soft_step, 1)
            nc.vector.tensor_tensor(logits, logits, maxima.unsqueeze(2).broadcast_to([M, BINS, N_CLASS]),
                                    ALU.subtract).then_inc(soft_step, 1)
            dve.wait_ge(exp_ready, 1)
            nc.vector.tensor_reduce(maxima, exps, AXIS.X, ALU.add).then_inc(soft_step, 1)
            dve.wait_ge(ln_ready, 1)
            nc.vector.tensor_tensor(logits, logits, stat[0:M, 1, :].unsqueeze(2).broadcast_to([M, BINS, N_CLASS]),
                                    ALU.subtract).then_inc(result_ready, 1)

        @block_ctx.tensor
        def _(pe):
            pe.wait_ge(consts_ready, 6)
            pe.wait_ge(counts_ready, 1)
            nc.tensor.matmul(ps[0:EP, BASE_BANK, 0:BINS], lower[0:EP, 0:EP], bin_stat[0:EP, 0, :], start=True, stop=True)
            nc.tensor.matmul(ps[:, BASE_BANK, 64:64 + BINS], ones[0:EP, :], bin_stat[0:EP, 0, :],
                             start=True, stop=True).then_inc(base_ready, 1)

            def scatter(g, s, first):
                pe.wait_ge(hot_ready, g + 1)
                for u in range(GROUP):
                    for f in range(N_FIELDS):
                        hot = hot_lo[0:EP, s, f, :, u]
                        last = nc.tensor.matmul(ps[:, FIELD_BANK + f, 0:TILES], hot.bitcast(BF16) if f < 3 else hot,
                                                hot_hi[0:EP, s, u, :], start=first and u == 0, stop=True,
                                                skip_group_check=True)
                last.then_inc(hot_used, 1)

            for g in range(2):
                scatter(g, g % 2, g == 0)
            with pe.Fori(2, EJ // GROUP, 2) as g:
                for u in range(2):
                    scatter(g + u, u, False)

            pe.wait_ge(slots_ready, 1)
            for layer in LAYERS:
                def pair(i, parity, start):
                    slot = pe.snap((i & 1) * 2)
                    for s in range(2):
                        pe.wait_ge(msg_lo_ready[layer], i * 2 + s + 1)
                        pe.wait_ge(row_hot_ready[layer], i * 2 + s + 1)
                        for part in (msg_hi, msg_lo):
                            for n in range(2):
                                last = nc.tensor.matmul(
                                    ps[:, SUM_BANK[parity] + n, :], row_hot[:, s, :],
                                    part[:, bass.ds(slot + s, 1), n * HALF:(n + 1) * HALF].rearrange("p o d -> p (o d)"),
                                    start=start and s == 0 and part is msg_hi, stop=True, skip_group_check=True)
                        last.then_inc(slot_free[layer], 1)

                conv_ready = (conv_lo_ready, conv_hi_ready[1])[layer]

                def turn(w, u):
                    q = w * UNITS[layer] + u
                    if not isinstance(q, int) or q >= 2:
                        pe.wait_ge(conv_ready, q - 1)
                    for k, (c, rows) in enumerate((c, rows) for c in unit_chunks(layer, u) for rows in (support, block)):
                        last = nc.tensor.transpose(ps[:, T_BANK + u % 2, k * P:k * P + M],
                                                   rows[:, c * P:(c + 1) * P], ident[0:M, 0:M])
                    last.then_inc(turned[layer], 1)

                def multiply(w, u):
                    pe.wait_ge(conv_ready, w * UNITS[layer] + u + 1)
                    if u == 0 and (not isinstance(w, int) or w >= 1):
                        pe.wait_ge(out_ready[layer], w)
                    for k, (c, of) in enumerate((c, of) for c in unit_chunks(layer, u) for of in range(2)):
                        if layer == 0:
                            hi, lo = conv_hi[:, u % 2, k, 0:M], conv_lo[:, u % 2, k, 0:M]
                            for x, y in ((hi, w_hi), (hi, w_lo), (lo, w_hi)):
                                for n in range(2):
                                    last = nc.tensor.matmul(
                                        ps[0:M, OUT_BANK + n, :], x, y[:, of * KC + c, n * HALF:(n + 1) * HALF],
                                        start=c == 0 and of == 0 and x is hi and y is w_hi, stop=True, skip_group_check=True)
                        else:
                            last = nc.tensor.matmul(ps[0:M, OUT_BANK, 0:N_CLASS], conv_f32[:, u % 2, k, 0:M],
                                                    w_out[:, of, c, :], start=c == 0 and of == 0, stop=True,
                                                    skip_group_check=True)
                    last.then_inc(unit_done[layer], 1)

                def step(b, parity, sums=True, multiplies=True):
                    if sums:
                        first, extra = bin_bounds(pe, b)
                        if not isinstance(b, int) or b >= 2:
                            pe.wait_ge(support_ready[layer], b - 1)
                        pair(first, parity, True)
                    for c in range(KC):
                        if sums:
                            portion(pe, first, extra, c, lambda i: pair(i, parity, False))
                        if multiplies:
                            if c == 0:
                                pe.wait_ge(support_ready[layer], b)
                                pe.wait_ge(product_ready[layer], b)
                            for u in MULTIPLY[layer].get(c, []):
                                multiply(b - 1, u)
                            for u in TURN[layer].get(c, []):
                                turn(b - 1, u)

                if layer == 0:
                    pe.wait_ge(w_lo_ready, 2 * KC)
                else:
                    pe.wait_ge(w_out_in, 32)
                step(0, 0, multiplies=False)
                step(1, 1)
                with pe.Fori(2, BINS, 2) as b:
                    b = b.with_bounds(min_val=2, max_val=BINS - 2)
                    step(b, 0)
                    step(b + 1, 1)
                step(BINS, 0, sums=False)


_INS = ["L0_rec_edge_row", "L0_rec_edge_col", "L0_rec_edge_val", "L0_rec_emb",
        "L0_rec_W1h", "L0_rec_W2h", "L0_rec_W1o", "L0_rec_W2o"]


def kernel(**inputs):
    import numpy as np
    import concourse.bacc as bacc
    from concourse.bass_utils import run_bass_kernel_spmd

    nc = bacc.Bacc("TRN2", target_bir_lowering=False, num_devices=1)
    arrays, args = {}, []
    for name in _INS:
        a = np.ascontiguousarray(inputs[name])
        arrays[f"in_{name}"] = a
        args.append(nc.dram_tensor(f"in_{name}", a.shape, mybir.dt.from_np(a.dtype), kind="ExternalInput").ap())
    out = nc.dram_tensor("out", (N_NODES, N_CLASS), F32, kind="ExternalOutput").ap()
    ngcf_kernel(nc, *args, out)
    return run_bass_kernel_spmd(nc, [arrays], core_ids=[0]).results[0]["out"]
```
